# Optimizing a Trainium2 kernel written in Bass

```python
import numpy as np
import jax
import jax.numpy as jnp

def _softmax(x, axis=-1):
    return jax.nn.softmax(x, axis=axis)

def _gelu(x):
    return jax.nn.gelu(x, approximate=True)

def _silu(x):
    return jax.nn.silu(x)

def _sigmoid(x):
    return jax.nn.sigmoid(x)

def _layernorm(x, axis=-1, eps=1e-05):
    m = jnp.mean(x, axis=axis, keepdims=True)
    v = jnp.var(x, axis=axis, keepdims=True)
    return (x - m) / jnp.sqrt(v + eps)

def _scatter_add(tgt, idx, src, axis=0):
    return tgt.at[idx].add(src)

def _segment_sum(src, seg, n):
    return jax.ops.segment_sum(src, seg, n)
kernel_name = 'mk_rec_standalone_d1_rec_r8_745814'

def setup_inputs(seed: int=0):
    np.random.seed(seed)
    _w = jnp.asarray

    def _rec_inputs():
        import jax
        import jax.numpy as jnp
        _rk = jax.random.key(seed)
        r_x0 = -0.000292821 + 1.00034 * jax.random.normal(jax.random.fold_in(_rk, 1), (512, 32, 64), jnp.float32)
        return r_x0
    r_x0 = _rec_inputs()

    def _L0_rec_setup():
        import jax, jax.numpy as jnp
        import numpy as np
        B, M, D = (256, 32, 64)
        SIZES = (128, 128, 128)

        def _cin(x0, Ws, bs):
            h = x0
            outs = []
            n = len(Ws)
            for i in range(n):
                H = h.shape[1]
                Wk = Ws[i].reshape(Ws[i].shape[0], H, M)
                xk = jax.nn.relu(jnp.einsum('bhd,bmd,ohm->bod', h, x0, Wk) + bs[i][None, :, None])
                if i != n - 1:
                    half = xk.shape[1] // 2
                    outs.append(xk[:, :half])
                    h = xk[:, half:]
                else:
                    outs.append(xk)
            return jnp.concatenate([o.sum(axis=-1) for o in outs], axis=1)
        key = jax.random.key(seed)
        ks = jax.random.split(key, 7)
        x0 = jax.random.normal(ks[0], (B, M, D), dtype=jnp.float32)
        inp = {'x0': x0}
        prev = M
        for i, s in enumerate(SIZES):
            inp[f'W{i + 1}'] = jax.random.normal(ks[1 + 2 * i], (s, prev * M), dtype=jnp.float32) * 0.05
            inp[f'b{i + 1}'] = jnp.zeros((s,), dtype=jnp.float32)
            prev = s // 2 if i != len(SIZES) - 1 else s
        return inp
    _L0_rec_all = _L0_rec_setup()
    _L0_rec_in = {k: v for k, v in _L0_rec_all.items() if k in ('W1', 'b1', 'W2', 'b2', 'W3', 'b3')}
    del _L0_rec_all
    return {'r_x0': r_x0, 'L0_rec_W1': _L0_rec_in['W1'], 'L0_rec_b1': _L0_rec_in['b1'], 'L0_rec_W2': _L0_rec_in['W2'], 'L0_rec_b2': _L0_rec_in['b2'], 'L0_rec_W3': _L0_rec_in['W3'], 'L0_rec_b3': _L0_rec_in['b3']}

def reference(r_x0, L0_rec_W1, L0_rec_b1, L0_rec_W2, L0_rec_b2, L0_rec_W3, L0_rec_b3):
    import jax
    import jax.numpy as jnp

    def _L0_rec_ref(x0, W1, b1, W2, b2, W3, b3):
        import jax, jax.numpy as jnp
        import numpy as np
        B, M, D = (256, 32, 64)
        SIZES = (128, 128, 128)

        def _cin(x0, Ws, bs):
            h = x0
            outs = []
            n = len(Ws)
            for i in range(n):
                H = h.shape[1]
                Wk = Ws[i].reshape(Ws[i].shape[0], H, M)
                xk = jax.nn.relu(jnp.einsum('bhd,bmd,ohm->bod', h, x0, Wk) + bs[i][None, :, None])
                if i != n - 1:
                    half = xk.shape[1] // 2
                    outs.append(xk[:, :half])
                    h = xk[:, half:]
                else:
                    outs.append(xk)
            return jnp.concatenate([o.sum(axis=-1) for o in outs], axis=1)
        return _cin(x0, (W1, W2, W3), (b1, b2, b3))
    y = _L0_rec_ref(r_x0, L0_rec_W1, L0_rec_b1, L0_rec_W2, L0_rec_b2, L0_rec_W3, L0_rec_b3)
    return y

_drawn_inputs = setup_inputs


def setup_inputs(seed=0):
    import zlib

    import numpy as np

    out = dict(_drawn_inputs(seed))
    spreads = {'L0_rec_b1': (0.0, 0.34), 'L0_rec_b2': (0.0, 0.398), 'L0_rec_b3': (0.0, 0.358)}
    factors = {}
    for name, (base, spread) in spreads.items():
        noise = np.random.default_rng([zlib.crc32(name.encode()), seed]).standard_normal(out[name].shape)
        drawn = base * np.exp(spread * noise) if base else spread * noise
        out[name] = jnp.asarray(drawn.astype(out[name].dtype))
    for name, factor in factors.items():
        out[name] = (out[name] * factor).astype(out[name].dtype)
    return out
```

```python
import concourse.bass as bass
from concourse import mybir
from contextlib import ExitStack
import numpy as np

B, M, D = 512, 32, 64
HID, OUT = 64, 128
TOK = B * D
T = 512
BT = T // D
TILES = TOK // T
BLK = 32
NB = 128 // BLK
XC = M // NB
C1 = 5
SUMMED = range(1, 13)
C23 = 2 * XC
G = 4
Q = C23 // G
GROUPS = [(False, 0, 0), (True, 1, 0), (False, 0, G), (True, 1, G)]
ORDER = [("mul", 1), ("mul", 0), ("low", 1), ("mul", 3), ("mul", 2), ("low", 3)]
XSLOTS, FSLOTS = 4, 3
FIRST, LAST = 4, TILES


def shift_rows():
    p = np.arange(128)
    s = NB * np.arange(XC)[None, :] + (p // BLK)[:, None]
    return (p % BLK)[:, None], ((p % BLK)[:, None] + s) % M


def cin_kernel(nc, xpad, w1, w1t, w2, w3, bias, ident_in, out):
    f32, f32r = mybir.dt.float32, mybir.dt.float32r
    ALU, ACT = mybir.AluOpType, mybir.ActivationFunctionType
    PLAIN = [q for q in range(Q) if not GROUPS[q][0]]
    SPLIT = [q for q in range(Q) if GROUPS[q][0]]
    NF, NS = len(PLAIN), len(SPLIT)

    ctx = ExitStack()
    with ctx:
        def sb(name, shape, dt=f32):
            return ctx.enter_context(nc.sbuf_tensor(name, shape, dt))

        def ps(name):
            return ctx.enter_context(nc.psum_tensor(name, [128, T], f32))

        def sem(name):
            return ctx.enter_context(nc.semaphore(name))

        W1 = sb("W1", [128, C1, OUT])
        WF = sb("WF", [128, 2, NF, G, OUT])
        WH = sb("WH", [128, 2, NS, G, OUT], f32r)
        WL = sb("WL", [128, 2, NS, G, OUT], f32r)
        bias_sb = sb("bias_sb", [128, 3])
        ident = sb("ident", [128, 128])
        X = sb("X", [128, XSLOTS, XC, T])
        XD = sb("XD", [128, 2, T])
        H = sb("H", [128, 2, 2, 2, T])
        ZF = sb("ZF", [128, FSLOTS, G, T])
        ZS = sb("ZS", [128, 2, G, T])
        ZH = sb("ZH", [128, 2, G, T], f32r)
        ZL = sb("ZL", [128, 2, G, T], f32r)
        R3 = sb("R3", [128, T])
        SUMS = sb("SUMS", [128, 3, B])
        OUTS = sb("OUTS", [128, B // 128, 2 * OUT])
        W1T = ZF[:, 0, :, 0:OUT]
        WS = ZS[:, :, 0:NS, :].rearrange("p w n (g o) -> p w n g o", g=G)

        ACC = [[ps(f"ACC{layer}{slot}") for slot in range(2)] for layer in range(3)]
        TR = [ps("TR0"), ps("TR1")]

        w1_loaded, w1t_loaded = sem("w1_loaded"), sem("w1t_loaded")
        ws_loaded, wf_loaded = sem("ws_loaded"), sem("wf_loaded")
        small_loaded = sem("small_loaded")
        w1_summed, w_high, w_low = sem("w1_summed"), sem("w_high"), sem("w_low")
        x_loaded = [sem(f"x_loaded{n}") for n in range(XSLOTS)]
        xd_loaded = [sem(f"xd_loaded{n}") for n in range(2)]
        plain_ready, plain_used = sem("plain_ready"), sem("plain_used")
        prod_ready, high_ready, low_ready = sem("prod_ready"), sem("high_ready"), sem("low_ready")
        split_used = sem("split_used")
        relu_done = [sem(f"relu_done{n}") for n in range(3)]
        h_copied = [[sem(f"h_copied{n}{s}") for s in range(2)] for n in range(2)]
        tr_done, outs_ready, stored = sem("tr_done"), sem("outs_ready"), sem("stored")

        block = ctx.enter_context(nc.Block())

        class Step:

            def __init__(self, i, at):
                self.i, self.at = i, at
                self.whole = FIRST <= at < LAST

            def tile(self, layer):
                at = self.at - layer
                return (self.i - layer, at) if self.whole or 0 <= at < TILES else None

            def plain_before(self, back=0):
                if self.whole:
                    return 6 * (self.i - back - 1), 6 * (self.at - back - 1)
                n = sum(NF * (0 <= k - layer < TILES) for k in range(self.at - back) for layer in range(3))
                return n, n

            def split_before(self):
                if self.whole:
                    return 4 * self.i - 6, 4 * self.at - 6
                n = sum(NS * (0 <= k - layer < TILES) for k in range(self.at) for layer in (1, 2))
                return n, n

            def plain(self, layer, q):
                here = NF * sum(self.tile(n) is not None for n in range(layer))
                n, at = self.plain_before()
                k = here + (q if layer == 0 else PLAIN.index(q))
                return n + k, (at + k) % FSLOTS

            def split(self, layer, q):
                n, at = self.split_before()
                k = NS * (layer == 2 and self.tile(1) is not None) + SPLIT.index(q)
                return n + k, (at + k) % 2

        def wide(ap):
            (p, c) = ap.ap
            return bass.AP(ap.tensor, ap.offset, [list(p), [0, G], list(c)])

        def steps(engine, body):
            for i in range(FIRST):
                body(Step(i, i))
            with engine.Fori(FIRST, LAST - XSLOTS + 1, XSLOTS) as i:
                for u in range(XSLOTS):
                    body(Step(i + u, FIRST + u))
            for i in range(LAST, TILES + 2):
                body(Step(i, i))

        @block.sync
        def _(sp):
            def load_x(t, at):
                slot = at % XSLOTS
                for k in range(NB):
                    src = bass.AP(xpad.tensor, k * TOK + t * T, [[TOK, BLK], [NB * TOK, XC], [1, T]])
                    sp.dma_start(X[BLK * k:BLK * k + BLK, slot, :, :], src).then_inc(x_loaded[slot], 16)

            def load_xd(t, at):
                for k in range(NB):
                    src = bass.AP(xpad.tensor, t * T, [[TOK, BLK], [1, T]])
                    sp.dma_start(XD[BLK * k:BLK * k + BLK, at % 2, :], src).then_inc(xd_loaded[at % 2], 16)

            def copy_hidden(layer, t, at):
                slot = at % 2
                sp.wait_ge(relu_done[layer], t + 1)
                lay0, lay1 = H[:, layer, slot, 0, :], H[:, layer, slot, 1, :]
                src = HID if layer == 0 else 0
                sp.dma_start(lay0[HID - src:2 * HID - src, :], lay0[src:src + HID, :]).then_inc(h_copied[layer][slot], 16)
                for p in range(0, 128, BLK):
                    half = src + (BLK if p % HID == 0 else 0)
                    sp.dma_start(lay1[p:p + BLK, :], lay0[half:half + BLK, :]).then_inc(h_copied[layer][slot], 16)

            load_xd(0, 0)
            load_x(0, 0)
            sp.dma_start(W1[:, :, :], w1).then_inc(w1_loaded, 16)
            sp.dma_start(W1T, w1t).then_inc(w1t_loaded, 16)
            for w, wd in enumerate((w2, w3)):
                for n, q in enumerate(SPLIT):
                    sp.dma_start(WS[:, w, n, :, :], wd[:, G * q:G * q + G, :]).then_inc(ws_loaded, 16)
            sp.dma_start(bias_sb[:, :], bias).then_inc(small_loaded, 16)
            sp.dma_start(ident[:, :], ident_in).then_inc(small_loaded, 16)
            for w, wd in enumerate((w2, w3)):
                for n, q in enumerate(PLAIN):
                    sp.dma_start(WF[:, w, n, :, :], wd[:, G * q:G * q + G, :]).then_inc(wf_loaded, 16)
            def body(step):
                if step.at + 1 < TILES:
                    if step.at >= 1:
                        sp.wait_ge(plain_ready, step.plain_before()[0])
                    load_xd(step.i + 1, step.at + 1)
                    load_x(step.i + 1, step.at + 1)
                for layer in (0, 1):
                    if step.tile(layer):
                        copy_hidden(layer, *step.tile(layer))

            steps(sp, body)
            for n in range(B // 128):
                sp.wait_ge(outs_ready, n + 1)
                sp.dma_start(out[128 * n:128 * n + 128, :], OUTS[:, n, :]).then_inc(stored, 16)
            sp.wait_ge(stored, 16 * (B // 128))

        @block.vector
        def _(dve):
            dve.wait_ge(w1_loaded, 16)
            dve.wait_ge(w1t_loaded, 16)
            for p0, p1, j0, j1 in ((32, 64, 0, 1), (64, 128, 0, 1), (0, 128, 1, 3), (0, 32, 3, 4)):
                w = W1[p0:p1, j0:j1, :]
                nc.vector.tensor_tensor(w, w, W1T[p0:p1, j0:j1, :], ALU.add).then_inc(w1_summed, 1)
            dve.wait_ge(w1_summed, 4)

            def plain_slot(step, layer, q):
                n, slot = step.plain(layer, q)
                if step.at >= FIRST or n >= FSLOTS:
                    dve.wait_ge(plain_used, n - FSLOTS + 1)
                return ZF[:, slot, :, :]

            def products(step):
                if step.tile(0):
                    t, at = step.tile(0)
                    dve.wait_ge(xd_loaded[at % 2], 16 * NB * (t // 2 + 1))
                    dve.wait_ge(x_loaded[at % XSLOTS], 16 * NB * (t // XSLOTS + 1))
                    x, xd = X[:, at % XSLOTS, :, :], XD[:, at % 2, :]
                    nc.vector.tensor_tensor(plain_slot(step, 0, 0), wide(xd), x[:, 0:G, :], ALU.mult)\
                        .then_inc(plain_ready, 1)
                    nc.vector.tensor_tensor(plain_slot(step, 0, 1)[:, 0, :], xd, x[:, G, :], ALU.mult)\
                        .then_inc(plain_ready, 1)
                for layer in (1, 2):
                    if not step.tile(layer):
                        continue
                    t, at = step.tile(layer)
                    dve.wait_ge(h_copied[layer - 1][at % 2], 16 * (1 + NB) * (t // 2 + 1))
                    for what, q in ORDER:
                        split, lay, j = GROUPS[q]
                        h, x = wide(H[:, layer - 1, at % 2, lay, :]), X[:, at % XSLOTS, j:j + G, :]
                        if not split:
                            nc.vector.tensor_tensor(plain_slot(step, layer, q), h, x, ALU.mult)\
                                .then_inc(plain_ready, 1)
                            continue
                        n, slot = step.split(layer, q)
                        later = step.at >= FIRST or n >= 2
                        if what == "mul":
                            if later:
                                dve.wait_ge(low_ready, n - 1)
                            nc.vector.tensor_tensor(ZS[:, slot, :, :], h, x, ALU.mult)\
                                .then_inc(prod_ready, 1)
                        else:
                            dve.wait_ge(high_ready, n + 1)
                            if later:
                                dve.wait_ge(split_used, n - 1)
                            nc.vector.tensor_tensor(ZL[:, slot, :, :], ZS[:, slot, :, :], ZH[:, slot, :, :],
                                                    ALU.subtract).then_inc(low_ready, 1)

            def body(step):
                if not step.whole and step.at == 1:
                    for w in range(2):
                        dve.wait_ge(w_high, w + 1)
                        nc.vector.tensor_tensor(WL[:, w, :, :, :], WS[:, w, :, :, :], WH[:, w, :, :, :],
                                                ALU.subtract).then_inc(w_low, 1)
                    dve.wait_ge(w_low, 2)
                products(step)

            steps(dve, body)
            for n in range(B // 128):
                dve.wait_ge(tr_done, n + 1)
                tr, o = TR[n % 2], OUTS[:, n, :]
                nc.vector.tensor_copy(o[:, 0:HID], tr[:, 0:HID])
                nc.vector.tensor_copy(o[:, HID:2 * HID], tr[:, OUT + HID:2 * OUT])
                nc.vector.tensor_copy(o[:, OUT:2 * OUT], tr[:, 2 * OUT:3 * OUT]).then_inc(outs_ready, 1)

        @block.scalar
        def _(act):
            act.wait_ge(ws_loaded, 16 * 2 * NS)
            for w in range(2):
                nc.scalar.activation(WH[:, w, :, :, :], WS[:, w, :, :, :], ACT.Copy).then_inc(w_high, 1)
            act.wait_ge(small_loaded, 32)

            def high(step, layer, q):
                n, slot = step.split(layer, q)
                if step.at >= FIRST or n >= 2:
                    act.wait_ge(split_used, n - 1)
                act.wait_ge(prod_ready, n + 1)
                nc.scalar.activation(ZH[:, slot, :, :], ZS[:, slot, :, :], ACT.Copy).then_inc(high_ready, 1)

            def relu(layer, t, at):
                to = R3[:, :] if layer == 2 else H[:, layer, at % 2, 0, :]
                for b in range(BT):
                    last = nc.scalar.activation(to[:, D * b:D * b + D], ACC[layer][at % 2][:, D * b:D * b + D], ACT.Relu,
                                                bias=bias_sb[:, layer:layer + 1],
                                                accum_out=SUMS[:, layer, bass.ds(BT * t + b, 1)])
                last.then_inc(relu_done[layer], 1)

            def body(step):
                if step.tile(1):
                    high(step, 1, SPLIT[0])
                if step.tile(3):
                    act.wait_ge(split_used, step.split_before()[0])
                    relu(2, *step.tile(3))
                if step.tile(0):
                    if step.at >= 2:
                        act.wait_ge(plain_ready, step.plain_before(1)[0] + 2 * NF)
                    act.wait_ge(plain_used, step.plain(0, 1)[0] + 1)
                    relu(0, *step.tile(0))
                if step.tile(1):
                    high(step, 1, SPLIT[1])
                if step.tile(2):
                    high(step, 2, SPLIT[0])
                if step.tile(1):
                    if step.at >= 3:
                        act.wait_ge(plain_ready, step.plain_before()[0])
                    act.wait_ge(split_used, step.split(1, Q - 1)[0] + 1)
                    relu(1, *step.tile(1))
                if step.tile(2):
                    high(step, 2, SPLIT[1])

            steps(act, body)
            body(Step(TILES + 2, TILES + 2))

        @block.tensor
        def _(pe):
            def body(step):
                for layer in range(3):
                    if not step.tile(layer):
                        continue
                    t, at = step.tile(layer)
                    acc = ACC[layer][at % 2]
                    first_use = not step.whole and t == 0
                    if step.at >= FIRST or t >= 2:
                        pe.wait_ge(relu_done[layer], t - 1)
                    if layer == 0:
                        if first_use:
                            pe.wait_ge(w1_summed, 4)
                        for q, chunks in enumerate((G, C1 - G)):
                            n, slot = step.plain(0, q)
                            pe.wait_ge(plain_ready, n + 1)
                            for g in range(chunks):
                                last = nc.tensor.matmul(acc[:, :], W1[:, G * q + g, :], ZF[:, slot, g, :],
                                                        start=(q == 0 and g == 0), stop=(q == 1))
                                if g == chunks - 1:
                                    last.then_inc(plain_used, 1)
                        continue
                    if first_use and layer == 1:
                        pe.wait_ge(wf_loaded, 16 * 2 * NF)
                        pe.wait_ge(w_low, 2)
                    w = layer - 1
                    for q in range(Q):
                        if not GROUPS[q][0]:
                            n, slot = step.plain(layer, q)
                            pe.wait_ge(plain_ready, n + 1)
                            for g in range(G):
                                last = nc.tensor.matmul(acc[:, :], WF[:, w, PLAIN.index(q), g, :], ZF[:, slot, g, :],
                                                        start=(q == 0 and g == 0), stop=False)
                            last.then_inc(plain_used, 1)
                            continue
                        n, slot = step.split(layer, q)
                        wh, wl = WH[:, w, SPLIT.index(q), :, :], WL[:, w, SPLIT.index(q), :, :]
                        pe.wait_ge(high_ready, n + 1)
                        for part in (wl, wh):
                            for g in range(G):
                                nc.tensor.matmul(acc[:, :], part[:, g, :], ZH[:, slot, g, :], start=False, stop=False)
                        pe.wait_ge(low_ready, n + 1)
                        for g in range(G):
                            last = nc.tensor.matmul(acc[:, :], wh[:, g, :], ZL[:, slot, g, :],
                                                    start=False, stop=(q == Q - 1 and g == G - 1))
                        last.then_inc(split_used, 1)

            steps(pe, body)
            pe.wait_ge(small_loaded, 32)
            for layer in range(3):
                pe.wait_ge(relu_done[layer], TILES)
            for n in range(B // 128):
                if n >= 2:
                    pe.wait_ge(outs_ready, n - 1)
                for layer in range(3):
                    last = nc.tensor.transpose(TR[n % 2][:, OUT * layer:OUT * layer + OUT],
                                               SUMS[:, layer, 128 * n:128 * n + 128], ident[:, :])
                last.then_inc(tr_done, 1)


def kernel(**inputs):
    import concourse.bacc as bacc
    from concourse.bass_utils import run_bass_kernel_spmd

    f = {k: np.asarray(v) for k, v in inputs.items()}
    hrow, xrow = shift_rows()
    x = f["r_x0"].transpose(1, 0, 2).reshape(M, TOK)
    xpad = np.concatenate([x, x], axis=0)
    w = f["L0_rec_W1"].reshape(OUT, M, M)
    w1 = w[:, hrow, xrow[:, :C1]].transpose(1, 2, 0)
    w1t = w[:, xrow[:, :G], hrow].transpose(1, 2, 0)
    upper_first = np.r_[HID:OUT, 0:HID]

    def arranged(w, order):
        w = w.reshape(OUT, HID, M)[order]
        half = (np.arange(128) // BLK)[:, None] % 2
        chunks = [w[:, (BLK * ((half + lay) % 2) + hrow), xrow[:, j:j + G]] for _, lay, j in GROUPS]
        return np.concatenate(chunks, axis=2).transpose(1, 2, 0)

    arrays = {
        "xpad": xpad, "w1": w1, "w1t": w1t,
        "w2": arranged(f["L0_rec_W2"], upper_first), "w3": arranged(f["L0_rec_W3"], np.arange(OUT)),
        "bias": np.stack([f["L0_rec_b1"], f["L0_rec_b2"][upper_first], f["L0_rec_b3"]], axis=1),
        "ident": np.eye(128, dtype=x.dtype),
    }
    arrays = {"in_" + k: np.ascontiguousarray(v) for k, v in arrays.items()}
    nc = bacc.Bacc("TRN2", target_bir_lowering=False, num_devices=1)
    args = [nc.dram_tensor(k, v.shape, mybir.dt.from_np(v.dtype), kind="ExternalInput").ap() for k, v in arrays.items()]
    args.append(nc.dram_tensor("out", (B, 2 * OUT), mybir.dt.float32, kind="ExternalOutput").ap())
    cin_kernel(nc, *args)
    return run_bass_kernel_spmd(nc, [arrays], core_ids=[0]).results[0]["out"]
```

```python
import concourse.bass as bass
from concourse import mybir
from contextlib import ExitStack
import numpy as np

B, M, D = 512, 32, 64
HID, OUT = 64, 128
TOK = B * D
T = 512
BT = T // D
TILES = TOK // T
BLK = 32
NB = 128 // BLK
XC = M // NB
C1 = 5
SUMMED = range(1, 13)
C23 = 2 * XC
G = 4
JG = G // 2
Q = C23 // G
PLAIN = 2
SPLIT = [0, 1, 3]
BY_POOL = {1: [0, 1], 2: [0, 3]}
BY_DVE = {1: [3], 2: [1]}
XSLOTS, WSLOTS, SSLOTS = 4, 2, 3
XP_SLOT = [0, 1, 2, 0, 1, 2, 0, 1]
FIRST, LAST = 4, TILES
ADDS = {
    "wide": (1, 1, 1),
    "split": (0, len(SPLIT), len(SPLIT)),
    "pool": (0, len(BY_POOL[1]), len(BY_POOL[2])),
    "dve": (0, len(BY_DVE[1]), len(BY_DVE[2])),
    "xp": (0, Q, Q),
}


def shift_rows():
    p = np.arange(128)
    s = NB * np.arange(XC)[None, :] + (p // BLK)[:, None]
    return (p % BLK)[:, None], ((p % BLK)[:, None] + s) % M


class Step:

    def __init__(self, i, at):
        self.i, self.at = i, at
        self.in_loop = not isinstance(i, int)

    def earlier(self, steps):
        return Step(self.i - steps, self.at - steps)

    def has(self, layer):
        return self.in_loop or 0 <= self.at - layer < TILES

    def tile(self, layer):
        return self.i - layer

    def before(self, what):
        adds = ADDS[what]
        if self.in_loop:
            per, less = sum(adds), sum(n * layer for layer, n in enumerate(adds))
            return self.i * per - less, self.at * per - less
        n = sum(adds[layer] * (0 <= k - layer < TILES) for k in range(self.at) for layer in range(3))
        return n, n

    def number(self, what, layer, k):
        k += sum(ADDS[what][below] for below in range(layer) if self.has(below))
        n, at = self.before(what)
        return n + k, at + k


def cin_kernel(nc, xpad, w1, w1t, w2, w3, bias, ident_in, out):
    f32, f32r = mybir.dt.float32, mybir.dt.float32r
    ALU, ACT, AX = mybir.AluOpType, mybir.ActivationFunctionType, mybir.AxisListType
    NS = len(SPLIT)

    ctx = ExitStack()
    with ctx:
        def sb(name, shape, dt=f32):
            return ctx.enter_context(nc.sbuf_tensor(name, shape, dt))

        def sem(name):
            return ctx.enter_context(nc.semaphore(name))

        W1 = sb("W1", [128, C1, OUT])
        WF = sb("WF", [128, 2, G, OUT])
        WH = sb("WH", [128, 2, NS, G, OUT], f32r)
        WL = sb("WL", [128, 2, NS, G, OUT], f32r)
        bias_sb = sb("bias_sb", [128, 3])
        ident = sb("ident", [128, 128])
        X = sb("X", [128, XSLOTS, XC, T])
        XD = sb("XD", [128, 2, T])
        H = [sb("H2", [128, 1, 2, T]), sb("H3", [128, 2, 2, T])]
        ZW = sb("ZW", [128, WSLOTS, G, T])
        ZN = sb("ZN", [128, T])
        ZS = sb("ZS", [128, SSLOTS, G, T])
        ZH = sb("ZH", [128, SSLOTS, G, T], f32r)
        ZL = sb("ZL", [128, SSLOTS, G, T], f32r)
        SUMS = sb("SUMS", [128, 3, B])
        W1T = ZW[:, 0, :, 0:OUT]
        WS = ZS[:, 0:2, 0:NS, :].rearrange("p w n (g o) -> p w n g o", g=G)
        OUTS = XD[:, :, :].rearrange("p a (b c) -> p (a b) c", b=2)

        ACC = [ctx.enter_context(nc.psum_tensor(f"ACC{n}", [128, T], f32)) for n in range(2)]
        XP = ctx.enter_context(nc.psum_tensor("XP", [128, 3, JG, T], f32))
        TR = [XP[:, n // JG, n % JG, :] for n in range(B // 128)]

        w1_loaded, w1t_loaded = sem("w1_loaded"), sem("w1t_loaded")
        ws_loaded = [sem("ws_loaded2"), sem("ws_loaded3")]
        wf_loaded = [sem("wf_loaded2"), sem("wf_loaded3")]
        small_loaded = sem("small_loaded")
        w1_summed, w_high, w_low = sem("w1_summed"), sem("w_high"), sem("w_low")
        x_loaded = [sem(f"x_loaded{n}") for n in range(XSLOTS)]
        xd_loaded = [sem(f"xd_loaded{n}") for n in range(2)]
        xp_ready = sem("xp_ready")
        wide_ready, wide_used = sem("wide_ready"), sem("wide_used")
        narrow_ready, narrow_used = sem("narrow_ready"), sem("narrow_used")
        prod_ready, high_ready = sem("prod_ready"), sem("high_ready")
        low_by_pool, low_by_dve = sem("low_by_pool"), sem("low_by_dve")
        split_used = sem("split_used")
        relu_done = [sem(f"relu_done{n}") for n in range(3)]
        summed = sem("summed")
        h_copied = [[sem("h_copied2")], [sem("h_copied3_0"), sem("h_copied3_1")]]
        tr_done, outs_ready, stored = sem("tr_done"), sem("outs_ready"), sem("stored")

        block = ctx.enter_context(nc.Block())

        def wait_product(engine, step, layer, q):
            if q == PLAIN:
                engine.wait_ge(wide_ready, step.number("wide", layer, 0)[0] + 1)
            else:
                engine.wait_ge(prod_ready, step.number("split", layer, SPLIT.index(q))[0] + 1)

        def wait_low(engine, step, layer, q):
            if q in BY_POOL[layer]:
                engine.wait_ge(low_by_pool, step.number("pool", layer, BY_POOL[layer].index(q))[0] + 1)
            else:
                engine.wait_ge(low_by_dve, step.number("dve", layer, BY_DVE[layer].index(q))[0] + 1)

        def wait_split_free(engine, step, layer, q):
            n, at = step.number("split", layer, SPLIT.index(q))
            if at >= SSLOTS:
                engine.wait_ge(split_used, n - SSLOTS + 1)

        def last_user(step, layer, key, same):
            users = [(step.earlier(back), l, k) for back in range(4) for l in (2, 1, 0) for k in reversed(range(Q))
                     if step.at >= back and step.earlier(back).has(l) and (back or (l, k) < (layer, key))]
            return next((u for u in users if same(*u)), None)

        def acc_of(step, layer):
            return (step.at + layer) % 2

        def steps(engine, body):
            for i in range(FIRST):
                body(Step(i, i))
            with engine.Fori(FIRST, LAST - XSLOTS + 1, XSLOTS) as i:
                for u in range(XSLOTS):
                    body(Step(i + u, FIRST + u))
            for i in range(LAST, TILES + 3):
                body(Step(i, i))

        @block.sync
        def _(sp):
            def load_x(t, at):
                slot = at % XSLOTS
                for k in range(NB):
                    src = bass.AP(xpad.tensor, k * TOK + t * T, [[TOK, BLK], [NB * TOK, XC], [1, T]])
                    sp.dma_start(X[BLK * k:BLK * k + BLK, slot, :, :], src).then_inc(x_loaded[slot], 16)

            def load_xd(t, at):
                for k in range(NB):
                    src = bass.AP(xpad.tensor, t * T, [[TOK, BLK], [1, T]])
                    sp.dma_start(XD[BLK * k:BLK * k + BLK, at % 2, :], src).then_inc(xd_loaded[at % 2], 16)

            def copy_hidden(step, layer):
                slots = h_copied[layer]
                slot = (step.at - layer) % len(slots)
                sp.wait_ge(relu_done[layer], step.tile(layer) + 1)
                lay0, lay1 = H[layer][:, slot, 0, :], H[layer][:, slot, 1, :]
                src = HID if layer == 0 else 0
                sp.dma_start(lay0[HID - src:2 * HID - src, :], lay0[src:src + HID, :]).then_inc(slots[slot], 16)
                for p in range(0, 128, BLK):
                    half = src + (BLK if p % HID == 0 else 0)
                    sp.dma_start(lay1[p:p + BLK, :], lay0[half:half + BLK, :]).then_inc(slots[slot], 16)

            sp.dma_start(W1[:, :, :], w1).then_inc(w1_loaded, 16)
            sp.dma_start(W1T, w1t).then_inc(w1t_loaded, 16)
            load_xd(0, 0)
            load_x(0, 0)
            sp.dma_start(bias_sb[:, :], bias).then_inc(small_loaded, 16)
            sp.dma_start(ident[:, :], ident_in).then_inc(small_loaded, 16)
            for w, wd in enumerate((w2, w3)):
                for n, q in enumerate(SPLIT):
                    sp.dma_start(WS[:, w, n, :, :], wd[:, G * q:G * q + G, :]).then_inc(ws_loaded[w], 16)
                sp.dma_start(WF[:, w, :, :], wd[:, G * PLAIN:G * PLAIN + G, :]).then_inc(wf_loaded[w], 16)

            def body(step):
                if step.in_loop or step.at + 1 < TILES:
                    if step.at >= 1:
                        sp.wait_ge(narrow_ready, step.i)
                        if step.at >= 3:
                            sp.wait_ge(xp_ready, step.before("xp")[0])
                    load_xd(step.i + 1, step.at + 1)
                    load_x(step.i + 1, step.at + 1)
                for layer in (0, 1):
                    if step.has(layer):
                        copy_hidden(step, layer)

            steps(sp, body)
            for n in range(B // 128):
                sp.wait_ge(outs_ready, n + 1)
                sp.dma_start(out[128 * n:128 * n + 128, :], OUTS[:, n, :]).then_inc(stored, 16)
            sp.wait_ge(stored, 16 * (B // 128))

        @block.vector
        def _(dve):
            dve.wait_ge(w1_loaded, 16)
            dve.wait_ge(w1t_loaded, 16)
            for p0, p1, j0, j1 in ((32, 64, 0, 1), (64, 128, 0, 1), (0, 128, 1, 3), (0, 32, 3, 4)):
                w = W1[p0:p1, j0:j1, :]
                nc.vector.tensor_tensor(w, w, W1T[p0:p1, j0:j1, :], ALU.add).then_inc(w1_summed, 1)
            dve.wait_ge(w1_summed, 4)

            def wide_slot(step, layer):
                n, at = step.number("wide", layer, 0)
                if at >= WSLOTS:
                    dve.wait_ge(wide_used, n - WSLOTS + 1)
                return ZW[:, at % WSLOTS, :, :]

            def layer1(step):
                t, at = step.tile(0), step.at
                dve.wait_ge(xd_loaded[at % 2], 16 * NB * (t // 2 + 1))
                dve.wait_ge(x_loaded[at % XSLOTS], 16 * NB * (t // XSLOTS + 1))
                x, xd = X[:, at % XSLOTS, :, :], XD[:, at % 2, :]
                p, c = xd.ap
                four = bass.AP(xd.tensor, xd.offset, [list(p), [0, G], list(c)])
                nc.vector.tensor_tensor(wide_slot(step, 0), four, x[:, 0:G, :], ALU.mult).then_inc(wide_ready, 1)
                if at >= 1:
                    dve.wait_ge(narrow_used, t)
                nc.vector.tensor_tensor(ZN[:, :], xd, x[:, G, :], ALU.mult).then_inc(narrow_ready, 1)

            def product(step, layer, q):
                t, at, slots = step.tile(layer), step.at - layer, h_copied[layer - 1]
                if q == 0:
                    dve.wait_ge(slots[at % len(slots)], 16 * (1 + NB) * (t // len(slots) + 1))
                dve.wait_ge(xp_ready, step.number("xp", layer, q)[0] + 1)
                h, x = H[layer - 1][:, at % len(slots), :, :], XP[:, XP_SLOT[Q * (layer - 1) + q], :, :]
                p, a, c = h.ap
                h = bass.AP(h.tensor, h.offset, [list(p), list(a), [0, JG], list(c)])
                p, j, c = x.ap
                x = bass.AP(x.tensor, x.offset, [list(p), [0, 2], list(j), list(c)])
                if q == PLAIN:
                    to, done = wide_slot(step, layer), wide_ready
                else:
                    at = step.number("split", layer, SPLIT.index(q))[1]
                    if at >= SSLOTS:
                        before = last_user(step, layer, q, lambda s, l, k: l and k in SPLIT
                                           and (at - s.number("split", l, SPLIT.index(k))[1]) % SSLOTS == 0)
                        wait_low(dve, *before)
                    to, done = ZS[:, at % SSLOTS, :, :], prod_ready
                to = to.rearrange("p (a j) t -> p a j t", a=2)
                nc.vector.tensor_tensor(to, h, x, ALU.mult).then_inc(done, 1)

            def low(step, layer, q):
                n, at = step.number("split", layer, SPLIT.index(q))
                wait_split_free(dve, step, layer, q)
                dve.wait_ge(high_ready, n + 1)
                nc.vector.tensor_tensor(ZL[:, at % SSLOTS, :, :], ZS[:, at % SSLOTS, :, :], ZH[:, at % SSLOTS, :, :],
                                        ALU.subtract).then_inc(low_by_dve, 1)

            def sums(step):
                dve.wait_ge(relu_done[2], step.tile(3) + 1)
                acc = ACC[acc_of(step.earlier(1), 2)][:, :]
                nc.vector.reduce_sum(SUMS[:, 2, bass.ds(BT * step.tile(3), BT)], acc.rearrange("p (b d) -> p b d", d=D),
                                     AX.X).then_inc(summed, 1)

            def gather(n):
                dve.wait_ge(tr_done, n + 1)
                tr, o = TR[n], OUTS[:, n, :]
                nc.vector.tensor_copy(o[:, 0:HID], tr[:, 0:HID])
                nc.vector.tensor_copy(o[:, HID:2 * HID], tr[:, OUT + HID:2 * OUT])
                nc.vector.tensor_copy(o[:, OUT:2 * OUT], tr[:, 2 * OUT:3 * OUT]).then_inc(outs_ready, 1)

            def body(step):
                if not step.in_loop and step.at == 1:
                    for w in range(2):
                        dve.wait_ge(w_high, w + 1)
                        nc.vector.tensor_tensor(WL[:, w, :, :, :], WS[:, w, :, :, :], WH[:, w, :, :, :],
                                                ALU.subtract).then_inc(w_low, 1)
                    dve.wait_ge(w_low, 2)
                if step.has(0):
                    layer1(step)
                for q in (0, 1, 2) if step.has(1) else ():
                    product(step, 1, q)
                if step.has(3) and step.has(1):
                    sums(step)
                if step.has(1):
                    product(step, 1, 3)
                if step.has(2):
                    product(step, 2, 0)
                if step.has(1):
                    low(step, 1, 3)
                if step.has(2):
                    for q in (1, 2, 3):
                        product(step, 2, q)
                    low(step, 2, 1)
                if step.has(3) and not step.has(1):
                    if not step.has(2):
                        for n in range(B // 128 - 1):
                            gather(n)
                    sums(step)

            steps(dve, body)
            gather(B // 128 - 1)

        @block.gpsimd
        def _(pool):
            def body(step):
                for layer in (1, 2):
                    for q in BY_POOL[layer] if step.has(layer) else ():
                        n, at = step.number("split", layer, SPLIT.index(q))
                        wait_split_free(pool, step, layer, q)
                        pool.wait_ge(high_ready, n + 1)
                        nc.gpsimd.tensor_tensor(ZL[:, at % SSLOTS, :, :], ZS[:, at % SSLOTS, :, :],
                                                ZH[:, at % SSLOTS, :, :], ALU.subtract).then_inc(low_by_pool, 1)

            steps(pool, body)

        @block.scalar
        def _(act):
            for w in range(2):
                act.wait_ge(ws_loaded[w], 16 * NS)
                nc.scalar.activation(WH[:, w, :, :, :], WS[:, w, :, :, :], ACT.Copy).then_inc(w_high, 1)
            act.wait_ge(small_loaded, 32)

            def copy_x(step, layer, q):
                slot, t = XP_SLOT[Q * (layer - 1) + q], step.tile(layer)
                before = last_user(step, layer, q, lambda s, l, k: l and XP_SLOT[Q * (l - 1) + k] == slot)
                if before:
                    wait_product(act, *before)
                if q == 0:
                    act.wait_ge(x_loaded[(step.at - layer) % XSLOTS], 16 * NB * (t // XSLOTS + 1))
                nc.scalar.activation(XP[:, slot, :, :], X[:, (step.at - layer) % XSLOTS, JG * q:JG * q + JG, :],
                                     ACT.Copy).then_inc(xp_ready, 1)

            def high(step, layer, q):
                n, at = step.number("split", layer, SPLIT.index(q))
                wait_split_free(act, step, layer, q)
                act.wait_ge(prod_ready, n + 1)
                nc.scalar.activation(ZH[:, at % SSLOTS, :, :], ZS[:, at % SSLOTS, :, :], ACT.Copy).then_inc(high_ready, 1)

            def relu_hidden(step, layer):
                slot = (step.at - layer) % len(h_copied[layer])
                acc, to = ACC[acc_of(step, layer)], H[layer][:, slot, 0, :]
                for b in range(BT):
                    last = nc.scalar.activation(to[:, D * b:D * b + D], acc[:, D * b:D * b + D], ACT.Relu,
                                                bias=bias_sb[:, layer:layer + 1],
                                                accum_out=SUMS[:, layer, bass.ds(BT * step.tile(layer) + b, 1)])
                last.then_inc(relu_done[layer], 1)

            def relu_last(step):
                act.wait_ge(split_used, step.before("split")[0])
                acc = ACC[acc_of(step.earlier(1), 2)][:, :]
                nc.scalar.activation(acc, acc, ACT.Relu, bias=bias_sb[:, 2:3]).then_inc(relu_done[2], 1)

            def relu_second(step):
                act.wait_ge(split_used, step.number("split", 1, NS - 1)[0] + 1)
                if step.at >= 3:
                    wait_product(act, step.earlier(1), 2, Q - 1)
                relu_hidden(step, 1)

            def body(step):
                if step.has(1):
                    for q in (0, 1, 2):
                        copy_x(step, 1, q)
                if not step.in_loop and step.at == 2:
                    relu_second(step.earlier(1))
                if step.has(1):
                    high(step, 1, 0)
                    copy_x(step, 1, 3)
                if step.has(3) and step.has(1):
                    relu_last(step)
                if step.has(1):
                    high(step, 1, 1)
                for q in (0, 1) if step.has(2) else ():
                    copy_x(step, 2, q)
                if step.has(1):
                    high(step, 1, 3)
                if step.has(0):
                    act.wait_ge(narrow_used, step.tile(0) + 1)
                    if step.has(1):
                        wait_product(act, step, 1, Q - 1)
                    relu_hidden(step, 0)
                if step.has(2):
                    copy_x(step, 2, 2)
                    high(step, 2, 0)
                    copy_x(step, 2, 3)
                    high(step, 2, 1)
                if step.has(1) and step.at >= 2:
                    relu_second(step)
                if step.has(2):
                    high(step, 2, 3)
                if step.has(3) and not step.has(1):
                    relu_last(step)

            steps(act, body)

        @block.tensor
        def _(pe):
            def free_acc(step, layer):
                before = last_user(step, layer, 0, lambda s, l, k: acc_of(s, l) == acc_of(step, layer))
                if before:
                    s, l, _ = before
                    pe.wait_ge(summed if l == 2 else relu_done[l], s.tile(l) + 1)
                return ACC[acc_of(step, layer)]

            def layer1(step):
                acc = free_acc(step, 0)
                if not step.in_loop and step.at == 0:
                    pe.wait_ge(w1_summed, 4)
                n, at = step.number("wide", 0, 0)
                pe.wait_ge(wide_ready, n + 1)
                for g in range(G):
                    last = nc.tensor.matmul(acc[:, :], W1[:, g, :], ZW[:, at % WSLOTS, g, :], start=(g == 0), stop=False)
                last.then_inc(wide_used, 1)
                pe.wait_ge(narrow_ready, step.tile(0) + 1)
                nc.tensor.matmul(acc[:, :], W1[:, G, :], ZN[:, :], start=False, stop=True).then_inc(narrow_used, 1)

            def plain(step, layer, acc):
                n, at = step.number("wide", layer, 0)
                pe.wait_ge(wide_ready, n + 1)
                for g in range(G):
                    last = nc.tensor.matmul(acc[:, :], WF[:, layer - 1, g, :], ZW[:, at % WSLOTS, g, :],
                                            start=(g == 0), stop=False)
                last.then_inc(wide_used, 1)

            def split(step, layer, acc, q):
                k = SPLIT.index(q)
                n, at = step.number("split", layer, k)
                wh, wl = WH[:, layer - 1, k, :, :], WL[:, layer - 1, k, :, :]
                pe.wait_ge(high_ready, n + 1)
                for part in (wl, wh):
                    for g in range(G):
                        nc.tensor.matmul(acc[:, :], part[:, g, :], ZH[:, at % SSLOTS, g, :], start=False, stop=False)
                wait_low(pe, step, layer, q)
                for g in range(G):
                    last = nc.tensor.matmul(acc[:, :], wh[:, g, :], ZL[:, at % SSLOTS, g, :],
                                            start=False, stop=(q == SPLIT[-1] and g == G - 1))
                last.then_inc(split_used, 1)

            def turn(n):
                if n == 0:
                    pe.wait_ge(small_loaded, 32)
                    for layer in (0, 1):
                        pe.wait_ge(relu_done[layer], TILES)
                    pe.wait_ge(summed, 128 * (B // 128 - 1) // BT)
                for layer in range(3):
                    last = nc.tensor.transpose(TR[n][:, OUT * layer:OUT * layer + OUT],
                                               SUMS[:, layer, 128 * n:128 * n + 128], ident[:, :])
                last.then_inc(tr_done, 1)

            def body(step):
                if step.has(0):
                    layer1(step)
                for layer in (1, 2):
                    if not step.has(layer):
                        continue
                    acc = free_acc(step, layer)
                    if not step.in_loop and step.at == layer:
                        pe.wait_ge(wf_loaded[layer - 1], 16)
                        pe.wait_ge(w_low, layer)
                    plain(step, layer, acc)
                    for q in SPLIT:
                        if not step.in_loop and step.at == TILES + 1 and q == SPLIT[-1]:
                            pe.wait_ge(prod_ready, step.number("split", 2, NS - 1)[0] + 1)
                            for n in range(B // 128 - 1):
                                turn(n)
                        split(step, layer, acc, q)

            steps(pe, body)
            pe.wait_ge(summed, TILES)
            turn(B // 128 - 1)


def kernel(**inputs):
    import concourse.bacc as bacc
    from concourse.bass_utils import run_bass_kernel_spmd

    f = {k: np.asarray(v) for k, v in inputs.items()}
    hrow, xrow = shift_rows()
    x = f["r_x0"].transpose(1, 0, 2).reshape(M, TOK)
    xpad = np.concatenate([x, x], axis=0)
    w = f["L0_rec_W1"].reshape(OUT, M, M)
    w1 = w[:, hrow, xrow[:, :C1]].transpose(1, 2, 0)
    w1t = w[:, xrow[:, :G], hrow].transpose(1, 2, 0)
    upper_first = np.r_[HID:OUT, 0:HID]

    def arranged(w, order):
        w = w.reshape(OUT, HID, M)[order]
        half = (np.arange(128) // BLK)[:, None] % 2
        chunks = [w[:, BLK * ((half + lay) % 2) + hrow, xrow[:, j:j + JG]] for j in range(0, XC, JG) for lay in (0, 1)]
        return np.concatenate(chunks, axis=2).transpose(1, 2, 0)

    arrays = {
        "xpad": xpad, "w1": w1, "w1t": w1t,
        "w2": arranged(f["L0_rec_W2"], upper_first), "w3": arranged(f["L0_rec_W3"], np.arange(OUT)),
        "bias": np.stack([f["L0_rec_b1"], f["L0_rec_b2"][upper_first], f["L0_rec_b3"]], axis=1),
        "ident": np.eye(128, dtype=x.dtype),
    }
    arrays = {"in_" + k: np.ascontiguousarray(v) for k, v in arrays.items()}
    nc = bacc.Bacc("TRN2", target_bir_lowering=False, num_devices=1)
    args = [nc.dram_tensor(k, v.shape, mybir.dt.from_np(v.dtype), kind="ExternalInput").ap() for k, v in arrays.items()]
    args.append(nc.dram_tensor("out", (B, 2 * OUT), mybir.dt.float32, kind="ExternalOutput").ap())
    cin_kernel(nc, *args)
    return run_bass_kernel_spmd(nc, [arrays], core_ids=[0]).results[0]["out"]
```
